# Optimizing a Trainium2 kernel written in Bass

```python
import numpy as np
import jax
import jax.numpy as jnp

def _softmax(x, axis=-1):
    return jax.nn.softmax(x, axis=axis)

def _gelu(x):
    return jax.nn.gelu(x, approximate=True)

def _silu(x):
    return jax.nn.silu(x)

def _sigmoid(x):
    return jax.nn.sigmoid(x)

def _layernorm(x, axis=-1, eps=1e-05):
    m = jnp.mean(x, axis=axis, keepdims=True)
    v = jnp.var(x, axis=axis, keepdims=True)
    return (x - m) / jnp.sqrt(v + eps)

def _scatter_add(tgt, idx, src, axis=0):
    return tgt.at[idx].add(src)

def _segment_sum(src, seg, n):
    return jax.ops.segment_sum(src, seg, n)
kernel_name = 'mk_dlrm_tower_d1_rec_r8_937e51'

def setup_inputs(seed: int=0):
    np.random.seed(seed)
    _w = jnp.asarray

    def _rec_inputs():
        import jax
        import jax.numpy as jnp
        _tk = jax.random.key(seed)
        ids = jnp.stack([jax.random.randint(jax.random.fold_in(_tk, 200 + f), (512,), 0, v, jnp.int32) for f, v in enumerate([1250, 1000, 1250, 125000, 12500, 1250, 1000, 1000, 12500, 12500, 1000, 1250, 12500, 1000, 12500, 1000, 1000, 1250, 12500, 12500, 1250, 1000, 1000, 12500, 1000, 1000])], axis=1)
        tbl_0 = 0.05 * jax.random.normal(jax.random.fold_in(_tk, 500 + 0), (1250, 128), jnp.float32)
        tbl_1 = 0.05 * jax.random.normal(jax.random.fold_in(_tk, 500 + 1), (1000, 128), jnp.float32)
        tbl_2 = 0.05 * jax.random.normal(jax.random.fold_in(_tk, 500 + 2), (1250, 128), jnp.float32)
        tbl_3 = 0.05 * jax.random.normal(jax.random.fold_in(_tk, 500 + 3), (125000, 128), jnp.float32)
        tbl_4 = 0.05 * jax.random.normal(jax.random.fold_in(_tk, 500 + 4), (12500, 128), jnp.float32)
        tbl_5 = 0.05 * jax.random.normal(jax.random.fold_in(_tk, 500 + 5), (1250, 128), jnp.float32)
        tbl_6 = 0.05 * jax.random.normal(jax.random.fold_in(_tk, 500 + 6), (1000, 128), jnp.float32)
        tbl_7 = 0.05 * jax.random.normal(jax.random.fold_in(_tk, 500 + 7), (1000, 128), jnp.float32)
        tbl_8 = 0.05 * jax.random.normal(jax.random.fold_in(_tk, 500 + 8), (12500, 128), jnp.float32)
        tbl_9 = 0.05 * jax.random.normal(jax.random.fold_in(_tk, 500 + 9), (12500, 128), jnp.float32)
        tbl_10 = 0.05 * jax.random.normal(jax.random.fold_in(_tk, 500 + 10), (1000, 128), jnp.float32)
        tbl_11 = 0.05 * jax.random.normal(jax.random.fold_in(_tk, 500 + 11), (1250, 128), jnp.float32)
        tbl_12 = 0.05 * jax.random.normal(jax.random.fold_in(_tk, 500 + 12), (12500, 128), jnp.float32)
        tbl_13 = 0.05 * jax.random.normal(jax.random.fold_in(_tk, 500 + 13), (1000, 128), jnp.float32)
        tbl_14 = 0.05 * jax.random.normal(jax.random.fold_in(_tk, 500 + 14), (12500, 128), jnp.float32)
        tbl_15 = 0.05 * jax.random.normal(jax.random.fold_in(_tk, 500 + 15), (1000, 128), jnp.float32)
        tbl_16 = 0.05 * jax.random.normal(jax.random.fold_in(_tk, 500 + 16), (1000, 128), jnp.float32)
        tbl_17 = 0.05 * jax.random.normal(jax.random.fold_in(_tk, 500 + 17), (1250, 128), jnp.float32)
        tbl_18 = 0.05 * jax.random.normal(jax.random.fold_in(_tk, 500 + 18), (12500, 128), jnp.float32)
        tbl_19 = 0.05 * jax.random.normal(jax.random.fold_in(_tk, 500 + 19), (12500, 128), jnp.float32)
        tbl_20 = 0.05 * jax.random.normal(jax.random.fold_in(_tk, 500 + 20), (1250, 128), jnp.float32)
        tbl_21 = 0.05 * jax.random.normal(jax.random.fold_in(_tk, 500 + 21), (1000, 128), jnp.float32)
        tbl_22 = 0.05 * jax.random.normal(jax.random.fold_in(_tk, 500 + 22), (1000, 128), jnp.float32)
        tbl_23 = 0.05 * jax.random.normal(jax.random.fold_in(_tk, 500 + 23), (12500, 128), jnp.float32)
        tbl_24 = 0.05 * jax.random.normal(jax.random.fold_in(_tk, 500 + 24), (1000, 128), jnp.float32)
        tbl_25 = 0.05 * jax.random.normal(jax.random.fold_in(_tk, 500 + 25), (1000, 128), jnp.float32)
        _rk = jax.random.fold_in(_tk, 7)
        r_dense_features = -0.000520686 + 1.00062 * jax.random.normal(jax.random.fold_in(_rk, 101), (512, 128), jnp.float32)
        W_top1 = 0.0405887 * jax.random.normal(jax.random.fold_in(_tk, 801), (607, 512), jnp.float32)
        W_top2 = 0.0441942 * jax.random.normal(jax.random.fold_in(_tk, 802), (512, 256), jnp.float32)
        W_top3 = 0.0625 * jax.random.normal(jax.random.fold_in(_tk, 803), (256, 1), jnp.float32)
        b_top1 = jnp.zeros((512,), jnp.float32)
        b_top2 = jnp.zeros((256,), jnp.float32)
        return (r_dense_features, ids, tbl_0, tbl_1, tbl_2, tbl_3, tbl_4, tbl_5, tbl_6, tbl_7, tbl_8, tbl_9, tbl_10, tbl_11, tbl_12, tbl_13, tbl_14, tbl_15, tbl_16, tbl_17, tbl_18, tbl_19, tbl_20, tbl_21, tbl_22, tbl_23, tbl_24, tbl_25, W_top1, b_top1, W_top2, b_top2, W_top3)
    r_dense_features, ids, tbl_0, tbl_1, tbl_2, tbl_3, tbl_4, tbl_5, tbl_6, tbl_7, tbl_8, tbl_9, tbl_10, tbl_11, tbl_12, tbl_13, tbl_14, tbl_15, tbl_16, tbl_17, tbl_18, tbl_19, tbl_20, tbl_21, tbl_22, tbl_23, tbl_24, tbl_25, W_top1, b_top1, W_top2, b_top2, W_top3 = _rec_inputs()

    def _L0_rec_setup():
        import jax, jax.numpy as jnp
        import numpy as np
        NUM_SPARSE = 26
        EMBED_DIM = 128
        BATCH = 2048
        key = jax.random.key(seed)
        k1, k2 = jax.random.split(key)
        dense_features = jax.random.normal(k1, (BATCH, EMBED_DIM), dtype=jnp.float32)
        sparse_features = jax.random.normal(k2, (BATCH, NUM_SPARSE, EMBED_DIM), dtype=jnp.float32)
        return {'dense_features': dense_features, 'sparse_features': sparse_features}
    _L0_rec_all = _L0_rec_setup()
    _L0_rec_in = {k: v for k, v in _L0_rec_all.items() if k in ()}
    del _L0_rec_all
    return {'r_dense_features': r_dense_features, 'ids': ids, 'tbl_0': tbl_0, 'tbl_1': tbl_1, 'tbl_2': tbl_2, 'tbl_3': tbl_3, 'tbl_4': tbl_4, 'tbl_5': tbl_5, 'tbl_6': tbl_6, 'tbl_7': tbl_7, 'tbl_8': tbl_8, 'tbl_9': tbl_9, 'tbl_10': tbl_10, 'tbl_11': tbl_11, 'tbl_12': tbl_12, 'tbl_13': tbl_13, 'tbl_14': tbl_14, 'tbl_15': tbl_15, 'tbl_16': tbl_16, 'tbl_17': tbl_17, 'tbl_18': tbl_18, 'tbl_19': tbl_19, 'tbl_20': tbl_20, 'tbl_21': tbl_21, 'tbl_22': tbl_22, 'tbl_23': tbl_23, 'tbl_24': tbl_24, 'tbl_25': tbl_25, 'W_top1': W_top1, 'b_top1': b_top1, 'W_top2': W_top2, 'b_top2': b_top2, 'W_top3': W_top3}

def reference(r_dense_features, ids, tbl_0, tbl_1, tbl_2, tbl_3, tbl_4, tbl_5, tbl_6, tbl_7, tbl_8, tbl_9, tbl_10, tbl_11, tbl_12, tbl_13, tbl_14, tbl_15, tbl_16, tbl_17, tbl_18, tbl_19, tbl_20, tbl_21, tbl_22, tbl_23, tbl_24, tbl_25, W_top1, b_top1, W_top2, b_top2, W_top3):
    import jax
    import jax.numpy as jnp

    def _L0_rec_ref(dense_features, sparse_features):
        import jax, jax.numpy as jnp
        import numpy as np
        NUM_SPARSE = 26
        EMBED_DIM = 128
        BATCH = 2048
        F = NUM_SPARSE + 1
        combined = jnp.concatenate([dense_features[:, None, :], sparse_features], axis=1)
        interactions = jnp.einsum('bfd,bgd->bfg', combined, combined)
        iu, ju = jnp.triu_indices(F, k=1)
        interactions_flat = interactions[:, iu, ju]
        return jnp.concatenate([dense_features, interactions_flat], axis=1)
    e = jnp.stack([tbl_0[ids[:, 0]], tbl_1[ids[:, 1]], tbl_2[ids[:, 2]], tbl_3[ids[:, 3]], tbl_4[ids[:, 4]], tbl_5[ids[:, 5]], tbl_6[ids[:, 6]], tbl_7[ids[:, 7]], tbl_8[ids[:, 8]], tbl_9[ids[:, 9]], tbl_10[ids[:, 10]], tbl_11[ids[:, 11]], tbl_12[ids[:, 12]], tbl_13[ids[:, 13]], tbl_14[ids[:, 14]], tbl_15[ids[:, 15]], tbl_16[ids[:, 16]], tbl_17[ids[:, 17]], tbl_18[ids[:, 18]], tbl_19[ids[:, 19]], tbl_20[ids[:, 20]], tbl_21[ids[:, 21]], tbl_22[ids[:, 22]], tbl_23[ids[:, 23]], tbl_24[ids[:, 24]], tbl_25[ids[:, 25]]], axis=1)
    z = _L0_rec_ref(r_dense_features, e)
    z = z.reshape(z.shape[0], -1)
    h = jnp.concatenate([z, r_dense_features], axis=1)
    h = jnp.maximum(h @ W_top1 + b_top1, 0.0)
    h = jnp.maximum(h @ W_top2 + b_top2, 0.0)
    y = h @ W_top3
    return y

_drawn_inputs = setup_inputs


def setup_inputs(seed=0):
    import zlib

    import numpy as np

    out = dict(_drawn_inputs(seed))
    spreads = {'b_top1': (0.0, 0.1), 'b_top2': (0.0, 0.1)}
    factors = {}
    for name, (base, spread) in spreads.items():
        noise = np.random.default_rng([zlib.crc32(name.encode()), seed]).standard_normal(out[name].shape)
        drawn = base * np.exp(spread * noise) if base else spread * noise
        out[name] = jnp.asarray(drawn.astype(out[name].dtype))
    for name, factor in factors.items():
        out[name] = (out[name] * factor).astype(out[name].dtype)
    return out
```

```python
from contextlib import ExitStack

import numpy as np

import concourse.bass as bass
from concourse import mybir

ALU = mybir.AluOpType
ACT = mybir.ActivationFunctionType
F32 = mybir.dt.float32
F32R = mybir.dt.float32r
I32 = mybir.dt.int32
U32 = mybir.dt.uint32

P = 128
BATCH, DIM, TABLES = 512, 128, 26
TILES = BATCH // P
FEATURES = TABLES + 1
H1, H2 = 512, 256
ROWS = [1250, 1000, 1250, 125000, 12500, 1250, 1000, 1000, 12500, 12500, 1000, 1250, 12500,
        1000, 12500, 1000, 1000, 1250, 12500, 12500, 1250, 1000, 1000, 12500, 1000, 1000]

ONEHOT = [1, 6, 7, 10, 13, 15, 16]
GATHERED = [t for t in range(TABLES) if t not in ONEHOT]
NOH, NG = len(ONEHOT), len(GATHERED)
CHUNKS = 8
OH_P = ROWS[ONEHOT[0]] // CHUNKS
PARTS = 2
SLOT_FEATURE = [0] + [1 + t for t in ONEHOT] + [1 + t for t in GATHERED]
SLOTS = 32
REACH = FEATURES // 2
VECTORS = REACH + 1
QUADS = P // 4
UNITS = [(0, 12), (12, 12), (24, 8)]
REGION = 3
BLOCKS = -(-VECTORS // 4)
GROUP = 4
GROUPS = [list(range(g, min(g + GROUP, NG))) for g in range(0, NG, GROUP)]
RING = 2
HALVES = 2


def block_partitions(r):
    return 32 * min(4, VECTORS - 4 * r)


def plan_steps():
    groups = [("group", t, g) for t in range(TILES) for g in range(len(GROUPS))]
    steps = [("prep", 0), ("prep", 1), ("dense",)]
    for i in range(NOH):
        steps.append(("onehot", i))
        if i + 2 < NOH:
            steps.append(("prep", i + 2))
        if i:
            steps.append(groups.pop(0))

    def take(t, n):
        out = [x for x in groups[:n] if x[1] <= t]
        del groups[:len(out)]
        return out

    for t in range(TILES):
        steps += take(t, len(GROUPS))
        steps += [("gram", t, 0)]
        if t:
            steps += [("layer1", t - 1, 0), ("layer1", t - 1, 1)]
        steps += [("gram", t, 1)]
        if t:
            steps += [("layer2", t - 1)]
        steps += take(t + 1, 2)
        steps += [("gram", t, 2)]
        steps += take(t + 1, 2)
    return steps + [("layer1", TILES - 1, 0), ("layer1", TILES - 1, 1), ("layer2", TILES - 1)]


STEPS = plan_steps()


def plan_ring():
    number, emptied_by = {}, {}
    for s in STEPS:
        if s[0] not in ("prep", "gram"):
            number[s] = len(number)
            emptied_by[s] = "scalar"
            if s[0] == "layer2" or (s[0] == "layer1" and s[2] == 1) or (s[0] == "group" and s[1] and s[2] % 2):
                emptied_by[s] = "vector"
    return number, emptied_by


USE, EMPTIED_BY = plan_ring()
USES = sorted(USE, key=USE.get)


def emptied(engine, last_use):
    return sum(EMPTIED_BY[s] == engine for s in USES[:last_use + 1])


def build(nc, dense, ids_cols, ids_rows, tables, w_pairs, w_dense_a, w_dense_b, b1, w2, b2, w3, out):
    ctx = ExitStack()
    with ctx:
        def sb(name, shape, dt=F32):
            return ctx.enter_context(nc.sbuf_tensor(name, shape, dt))

        def sem(name):
            return ctx.enter_context(nc.semaphore(name))

        idx = sb("idx", [P, TILES * TABLES], I32)
        ids_bc = sb("ids_bc", [P, 2, BATCH], I32)
        first_row = sb("first_row", [P, 1])
        ident = sb("ident", [P, P])
        dense_sb = sb("dense_sb", [P, TILES, DIM])
        gath = sb("gath", [P, 2, NG, DIM])
        xT = sb("xT", [P, BATCH, SLOTS])
        table = sb("table", [P, 2, CHUNKS * DIM])
        parts = sb("parts", [P, 2, PARTS, CHUNKS * DIM], F32R)
        offset = sb("offset", [P, 2, BATCH])
        onehot = sb("onehot", [P, 2, CHUNKS, BATCH], F32R)
        overlaid = sb("overlaid", [P, REACH], I32)
        pairs = sb("pairs", [P, 2, BLOCKS, P])
        wp = sb("wp", [P, BLOCKS, H1])
        wd = sb("wd", [P, 3, H1])
        denseT = sb("denseT", [P, BATCH])
        b1_sb = sb("b1_sb", [P, H1 // P])
        w2_sb = sb("w2_sb", [P, H1 // P, H2])
        b2_bc = sb("b2_bc", [P, H2])
        w3_bc = sb("w3_bc", [P, H2])
        h1T = sb("h1T", [P, 2, H1 // P, P])
        h2 = sb("h2", [P, H2])
        h2w = sb("h2w", [P, H2])
        y = sb("y", [P, TILES])

        bank = [ctx.enter_context(nc.psum_tensor(f"bank{i}", [P, 512], F32)) for i in range(RING)]
        gram = [ctx.enter_context(nc.psum_tensor(f"gram{i}", [P, 4 * REGION, P], F32)) for i in range(2)]

        idx_loaded = sem("idx_loaded")
        ids_loaded = [sem(f"ids_loaded{i}") for i in range(NOH)]
        table_loaded = [sem(f"table_loaded{i}") for i in range(NOH)]
        dense_loaded = sem("dense_loaded")
        wd_loaded = sem("wd_loaded")
        wp_loaded = sem("wp_loaded")
        b1_loaded = sem("b1_loaded")
        w2_loaded = sem("w2_loaded")
        b2_loaded = sem("b2_loaded")
        w3_loaded = sem("w3_loaded")
        rows_in = [[sem(f"rows_in{p}_{g}") for g in range(len(GROUPS))] for p in range(2)]
        ident_zeroed = sem("ident_zeroed")
        ident_ready = sem("ident_ready")
        first_row_ready = sem("first_row_ready")
        pads_zeroed = sem("pads_zeroed")
        wd_summed = sem("wd_summed")
        offset_ready = sem("offset_ready")
        onehots_ready = sem("onehots_ready")
        high_ready = sem("high_ready")
        parts_ready = sem("parts_ready")
        half_used = sem("half_used")
        bank_full = sem("bank_full")
        freed = {"scalar": sem("freed_by_scalar"), "vector": sem("freed_by_vector")}
        gram_full = sem("gram_full")
        base_copied = sem("base_copied")
        mask_filled = sem("mask_filled")
        mask_ready = sem("mask_ready")
        pairs_ready = sem("pairs_ready")
        denseT_copied = sem("denseT_copied")
        h2_biased = sem("h2_biased")
        y_ready = sem("y_ready")
        y_stored = sem("y_stored")

        block = ctx.enter_context(nc.Block())

        @block.sync
        def _(sp):
            sp.dma_start(idx[:], ids_cols).then_inc(idx_loaded, 16)

            def load_table(i):
                if i >= 2:
                    sp.wait_ge(parts_ready, HALVES * (i - 1))
                    sp.wait_ge(offset_ready, i - 1)
                sp.dma_start(table[0:OH_P, i % 2, :],
                             tables[ONEHOT[i]].rearrange("(p c) d -> p (c d)", c=CHUNKS)
                             ).then_inc(table_loaded[i], 16)
                sp.dma_start(ids_bc[0:OH_P, i % 2, :], ids_rows[i:i + 1, :].broadcast_to([OH_P, BATCH])
                             ).then_inc(ids_loaded[i], 16)

            load_table(0)
            load_table(1)
            sp.dma_start(dense_sb[:], dense).then_inc(dense_loaded, 16)
            sp.dma_start(wd[:, 0, :], w_dense_a).then_inc(wd_loaded, 16)
            sp.dma_start(wd[:, 1, :], w_dense_b).then_inc(wd_loaded, 16)
            load_table(2)
            sp.dma_start(wp[:, 0:BLOCKS - 1, :], w_pairs[:, 0:BLOCKS - 1, :]).then_inc(wp_loaded, 16)
            last = block_partitions(BLOCKS - 1)
            sp.dma_start(wp[0:last, BLOCKS - 1, :], w_pairs[0:last, BLOCKS - 1, :]).then_inc(wp_loaded, 16)
            for i in range(3, NOH):
                load_table(i)
            sp.dma_start(b1_sb[:], b1).then_inc(b1_loaded, 16)
            sp.dma_start(w2_sb[:], w2).then_inc(w2_loaded, 16)
            sp.dma_start(b2_bc[:], b2.broadcast_to([P, H2])).then_inc(b2_loaded, 16)
            sp.dma_start(w3_bc[:], w3.broadcast_to([P, H2])).then_inc(w3_loaded, 16)
            for t in range(TILES):
                sp.wait_ge(y_ready, t + 1)
                sp.dma_start(out[t * P:(t + 1) * P, :], y[:, t:t + 1]).then_inc(y_stored, 16)
            sp.wait_ge(y_stored, 16 * TILES)

        @block.gpsimd
        def _(pool):
            nc.gpsimd.memset(ident[:], 0.0).then_inc(ident_zeroed, 1)
            nc.gpsimd.iota(first_row[:], [[0, 1]], base=0, channel_multiplier=CHUNKS,
                           allow_small_or_imprecise_dtypes=True).then_inc(first_row_ready, 1)
            pool.wait_ge(ident_zeroed, 1)
            nc.gpsimd.affine_select(out=ident[:], in_=ident[:], compare_op=ALU.not_equal, fill=1.0, base=0,
                                    pattern=[[-1, P]], channel_multiplier=1).then_inc(ident_ready, 1)
            for j in range(4):
                mask = overlaid[32 * j:32 * j + 32, :]
                nc.gpsimd.memset(mask, 1).then_inc(mask_filled, 1)
                pool.wait_ge(mask_filled, 3 * j + 1)
                nc.gpsimd.affine_select(out=mask, in_=mask, compare_op=ALU.is_gt, fill=0.0, base=0,
                                        pattern=[[-1, REACH]], channel_multiplier=1).then_inc(mask_filled, 1)
                pool.wait_ge(mask_filled, 3 * j + 2)
                nc.gpsimd.affine_select(out=mask, in_=mask, compare_op=ALU.is_ge, fill=0.0, base=REACH,
                                        pattern=[[1, REACH]], channel_multiplier=-1).then_inc(mask_filled, 1)
                pool.wait_ge(mask_filled, 3 * j + 3)
                pool.sem_inc(mask_ready, 1)
            pool.wait_ge(idx_loaded, 16)
            for t in range(TILES):
                for g, group in enumerate(GROUPS):
                    if t >= 2:
                        pool.wait_ge(bank_full, USE[("group", t - 2, g)] + 1)
                    for s in group:
                        nc.gpsimd.indirect_dma_start(
                            gath[:, t % 2, s, :], None, tables[GATHERED[s]],
                            bass.IndirectOffsetOnAxis(
                                idx[:, t * TABLES + GATHERED[s]:t * TABLES + GATHERED[s] + 1].bitcast(U32), 0),
                        ).then_inc(rows_in[t % 2][g], 16)

        def pair_blocks(s):
            _, t, u = s
            first_quad, quads = UNITS[u]
            products = gram[(t * len(UNITS) + u) % 2]
            for j in range(4):
                for k in range(4):
                    base = list(range(k, VECTORS, 4))
                    over = list(range(k, REACH, 4))
                    b0 = 4 * first_quad + j
                    at = slice(b0, b0 + 4 * (quads - 1) + 1, 4)

                    def columns(vectors, shift):
                        c = FEATURES * j + vectors[0] + shift
                        return products[32 * j:32 * j + 32, 0:quads, c:c + 4 * (len(vectors) - 1) + 1:4
                                        ].rearrange("p q r -> p r q")

                    dst = pairs[32 * k:32 * k + 32, t % 2, :, :]
                    mask = overlaid[32 * j:32 * j + 32, k:over[-1] + 1:4].unsqueeze(2).broadcast_to(
                        [32, len(over), quads])
                    yield (dst[:, 0:len(base), at], columns(base, REACH),
                           dst[:, 0:len(over), at], columns(over, 0), mask)

        def feature_bank(s):
            src = bank[USE[s] % RING]
            if s[0] == "dense":
                return xT[:, :, 0], src[:]
            if s[0] == "onehot":
                return xT[:, :, 1 + s[1]], src[:]
            _, t, g = s
            s0, n = 1 + NOH + GROUPS[g][0], len(GROUPS[g])
            return (xT[:, t * P:(t + 1) * P, s0:s0 + n].rearrange("p b s -> p s b"),
                    src[:, 0:n * P].rearrange("p (s b) -> p s b", s=n))

        def hidden(s):
            _, t, half = s
            for n in range(H1 // P // HALVES):
                c = half * (H1 // P // HALVES) + n
                yield h1T[:, t % 2, c, :], bank[USE[s] % RING][:, n * P:(n + 1) * P], b1_sb[:, c:c + 1]

        @block.scalar
        def _(act):
            for s in STEPS:
                if s in USE and EMPTIED_BY[s] == "scalar":
                    act.wait_ge(bank_full, USE[s] + 1)
                if s[0] == "prep":
                    i = s[1]
                    act.wait_ge(table_loaded[i], 16)
                    for half in range(HALVES):
                        if i >= 2:
                            if half == 0:
                                act.wait_ge(half_used, i - 1)
                            else:
                                act.wait_ge(bank_full, USE[("onehot", i - 2)] + 1)
                        c = slice(half * CHUNKS * DIM // HALVES, (half + 1) * CHUNKS * DIM // HALVES)
                        nc.scalar.copy(parts[0:OH_P, i % 2, 0, c], table[0:OH_P, i % 2, c]).then_inc(high_ready, 1)
                elif s[0] == "gram":
                    n = len(UNITS) * s[1] + s[2]
                    act.wait_ge(gram_full, n + 1)
                    if s[1] >= 2 and s[2] == 0:
                        act.wait_ge(bank_full, USE[("layer1", s[1] - 2, 1)] + 1)
                    for m, (dst, src, *_) in enumerate(pair_blocks(s)):
                        last = nc.scalar.copy(dst, src)
                        if m % 4 == 3:
                            last.then_inc(base_copied, 1)
                elif s[0] == "layer1" and EMPTIED_BY[s] == "scalar":
                    if s == ("layer1", 0, 0):
                        act.wait_ge(b1_loaded, 16)
                    if s[1] >= 2:
                        act.wait_ge(bank_full, USE[("layer2", s[1] - 2)] + 1)
                    for dst, src, bias in hidden(s):
                        last = nc.scalar.activation(dst, src, ACT.Relu, bias=bias)
                    last.then_inc(freed["scalar"], 1)
                elif s in USE and EMPTIED_BY[s] == "scalar":
                    if s[0] == "dense":
                        nc.scalar.copy(denseT[:], bank[USE[s] % RING][:]).then_inc(denseT_copied, 1)
                    dst, src = feature_bank(s)
                    nc.scalar.copy(dst, src).then_inc(freed["scalar"], 1)

        @block.vector
        def _(dve):
            nc.vector.memset(xT[:, :, FEATURES:SLOTS], 0.0).then_inc(pads_zeroed, 1)
            dve.wait_ge(first_row_ready, 1)
            for s in STEPS:
                if s in USE and EMPTIED_BY[s] == "vector":
                    dve.wait_ge(bank_full, USE[s] + 1)
                if s[0] == "prep":
                    i = s[1]
                    b = i % 2
                    dve.wait_ge(ids_loaded[i], 16)
                    nc.vector.tensor_scalar(offset[0:OH_P, b, :], ids_bc[0:OH_P, b, :], first_row[0:OH_P, :],
                                            None, ALU.subtract).then_inc(offset_ready, 1)
                    dve.wait_ge(offset_ready, i + 1)
                    for half in range(HALVES):
                        if i >= 2:
                            if half == 0:
                                dve.wait_ge(half_used, i - 1)
                            else:
                                dve.wait_ge(bank_full, USE[("onehot", i - 2)] + 1)
                        for c in range(half * CHUNKS // HALVES, (half + 1) * CHUNKS // HALVES):
                            last = nc.vector.tensor_scalar(onehot[0:OH_P, b, c, :], offset[0:OH_P, b, :], float(c),
                                                           None, ALU.is_equal)
                        last.then_inc(onehots_ready, 1)
                        dve.wait_ge(high_ready, HALVES * i + half + 1)
                        c = slice(half * CHUNKS * DIM // HALVES, (half + 1) * CHUNKS * DIM // HALVES)
                        nc.vector.tensor_tensor(parts[0:OH_P, b, 1, c], table[0:OH_P, b, c],
                                                parts[0:OH_P, b, 0, c].bitcast(F32), ALU.subtract
                                                ).then_inc(parts_ready, 1)
                elif s[0] == "gram":
                    n = len(UNITS) * s[1] + s[2]
                    if n == 0:
                        dve.wait_ge(mask_ready, 4)
                    for m, (_, _, dst, src, mask) in enumerate(pair_blocks(s)):
                        if m % 4 == 0:
                            dve.wait_ge(base_copied, 4 * n + m // 4 + 1)
                        last = nc.vector.copy_predicated(dst, mask, src)
                    last.then_inc(pairs_ready, 1)
                elif s[0] == "layer1" and EMPTIED_BY[s] == "vector":
                    if s == ("layer1", 0, 1):
                        dve.wait_ge(b1_loaded, 16)
                    if s[1] >= 2:
                        dve.wait_ge(bank_full, USE[("layer2", s[1] - 2)] + 1)
                    for dst, src, bias in hidden(s):
                        last = nc.vector.tensor_scalar(dst, src, bias, 0.0, ALU.add, ALU.max)
                    last.then_inc(freed["vector"], 1)
                elif s[0] == "layer2":
                    t = s[1]
                    if t == 0:
                        dve.wait_ge(b2_loaded, 16)
                        dve.wait_ge(w3_loaded, 16)
                    else:
                        dve.wait_ge(y_ready, t)
                    nc.vector.tensor_tensor(h2[:], bank[USE[s] % RING][:, 0:H2], b2_bc[:], ALU.add
                                            ).then_inc(freed["vector"], 1)
                    dve.wait_ge(freed["vector"], emptied("vector", USE[s]))
                    nc.vector.scalar_tensor_tensor(out=h2w[:], in0=h2[:], scalar=0.0, in1=w3_bc[:], op0=ALU.max,
                                                   op1=ALU.mult, accum_out=y[:, t:t + 1]).then_inc(y_ready, 1)
                elif s in USE and EMPTIED_BY[s] == "vector":
                    dst, src = feature_bank(s)
                    nc.vector.tensor_copy(dst, src).then_inc(freed["vector"], 1)
                if s == ("dense",):
                    dve.wait_ge(wd_loaded, 32)
                    nc.vector.tensor_tensor(wd[:, 2, :], wd[:, 0, :], wd[:, 1, :], ALU.add).then_inc(wd_summed, 1)

        @block.tensor
        def _(pe):
            def wait_emptied(last_use):
                for engine in freed:
                    if emptied(engine, last_use):
                        pe.wait_ge(freed[engine], emptied(engine, last_use))

            pe.wait_ge(ident_ready, 1)
            for s in STEPS:
                if s in USE:
                    dst = bank[USE[s] % RING]
                    if USE[s] >= RING:
                        wait_emptied(USE[s] - RING)
                if s[0] == "dense":
                    pe.wait_ge(dense_loaded, 16)
                    for t in range(TILES):
                        last = nc.tensor.transpose(dst[:, t * P:(t + 1) * P], dense_sb[:, t, :], ident[:])
                    last.then_inc(bank_full, 1)
                elif s[0] == "onehot":
                    i = s[1]
                    for c in range(CHUNKS):
                        if c % (CHUNKS // HALVES) == 0:
                            half = HALVES * i + c // (CHUNKS // HALVES)
                            pe.wait_ge(onehots_ready, half + 1)
                            pe.wait_ge(parts_ready, half + 1)
                        for part in range(PARTS):
                            last = nc.tensor.matmul(dst[:], parts[0:OH_P, i % 2, part, c * DIM:(c + 1) * DIM],
                                                    onehot[0:OH_P, i % 2, c, :],
                                                    start=(c == 0 and part == 0),
                                                    stop=(c == CHUNKS - 1 and part == PARTS - 1))
                        if c == CHUNKS // HALVES - 1:
                            last.then_inc(half_used, 1)
                    last.then_inc(bank_full, 1)
                elif s[0] == "group":
                    _, t, g = s
                    pe.wait_ge(rows_in[t % 2][g], 16 * len(GROUPS[g]) * (t // 2 + 1))
                    for n, slot in enumerate(GROUPS[g]):
                        last = nc.tensor.transpose(dst[:, n * P:(n + 1) * P], gath[:, t % 2, slot, :], ident[:])
                    last.then_inc(bank_full, 1)
                elif s[0] == "gram":
                    _, t, u = s
                    n = len(UNITS) * t + u
                    if n == 0:
                        pe.wait_ge(pads_zeroed, 1)
                    if u == 0:
                        wait_emptied(max(USE[x] for x in USE if x[0] in ("dense", "onehot") or
                                         (x[0] == "group" and x[1] == t)))
                    if n >= 2:
                        pe.wait_ge(pairs_ready, n - 1)
                    first_quad, quads = UNITS[u]
                    for q in range(quads):
                        b0 = t * P + 4 * (first_quad + q)
                        quad = xT[:, b0:b0 + 4, :]
                        last = nc.tensor.matmul(gram[n % 2][:, q, 0:4 * FEATURES], quad, quad[:, :, 0:FEATURES],
                                                start=True, stop=True)
                    last.then_inc(gram_full, 1)
                elif s[0] == "layer1":
                    _, t, half = s
                    if t == 0:
                        pe.wait_ge(wd_summed, 1)
                        pe.wait_ge(denseT_copied, 1)
                        pe.wait_ge(wp_loaded, 32)
                    pe.wait_ge(pairs_ready, len(UNITS) * (t + 1))
                    for n in range(H1 // P // HALVES):
                        h = slice((half * (H1 // P // HALVES) + n) * P, (half * (H1 // P // HALVES) + n + 1) * P)
                        to = dst[:, n * P:(n + 1) * P]
                        nc.tensor.matmul(to, wd[:, 2, h], denseT[:, t * P:(t + 1) * P], start=True, stop=False)
                        for r in range(BLOCKS):
                            k = block_partitions(r)
                            last = nc.tensor.matmul(to, wp[0:k, r, h], pairs[0:k, t % 2, r, :],
                                                    start=False, stop=(r == BLOCKS - 1))
                    last.then_inc(bank_full, 1)
                elif s[0] == "layer2":
                    t = s[1]
                    if t == 0:
                        pe.wait_ge(w2_loaded, 16)
                    wait_emptied(USE[("layer1", t, 1)])
                    for c in range(H1 // P):
                        last = nc.tensor.matmul(dst[:, 0:H2], h1T[:, t % 2, c, :], w2_sb[:, c, :],
                                                start=(c == 0), stop=(c == H1 // P - 1))
                    last.then_inc(bank_full, 1)


def pair_rows():
    first = np.cumsum([0] + [FEATURES - 1 - f for f in range(FEATURES - 1)])
    rows = np.full((P, BLOCKS), -1)
    for m in range(VECTORS):
        for slot in range(FEATURES):
            column = m if m < slot <= m + REACH and m < REACH else m + REACH
            if (slot - column) % FEATURES in range(1, REACH + 1):
                lo, hi = sorted((SLOT_FEATURE[slot], SLOT_FEATURE[column]))
                rows[32 * (m % 4) + slot, m // 4] = DIM + first[lo] + hi - lo - 1
    assert sorted(rows[rows >= 0]) == list(range(DIM, DIM + FEATURES * REACH))
    return rows


def kernel(**inputs):
    import concourse.bacc as bacc
    from concourse.bass_utils import run_bass_kernel_spmd

    w1 = np.asarray(inputs["W_top1"])
    ids = np.asarray(inputs["ids"])
    rows = pair_rows()
    w_pairs = np.zeros((P, BLOCKS, H1), w1.dtype)
    w_pairs[rows >= 0] = w1[rows[rows >= 0]]
    arrays = {
        "dense": np.asarray(inputs["r_dense_features"]).reshape(TILES, P, DIM).transpose(1, 0, 2),
        "ids_cols": ids.reshape(TILES, P, TABLES).transpose(1, 0, 2).reshape(P, TILES * TABLES),
        "ids_rows": ids.T[ONEHOT],
        **{f"tbl_{t}": np.asarray(inputs[f"tbl_{t}"]) for t in range(TABLES)},
        "w_pairs": w_pairs,
        "w_dense_a": w1[:DIM],
        "w_dense_b": w1[-DIM:],
        "b1": np.asarray(inputs["b_top1"]).reshape(H1 // P, P).T,
        "w2": np.asarray(inputs["W_top2"]).reshape(H1 // P, P, H2).transpose(1, 0, 2),
        "b2": np.asarray(inputs["b_top2"]).reshape(1, H2),
        "w3": np.asarray(inputs["W_top3"]).reshape(1, H2),
    }
    arrays = {f"in_{k}": np.ascontiguousarray(v) for k, v in arrays.items()}
    nc = bacc.Bacc("TRN2", target_bir_lowering=False, num_devices=1)
    aps = {k[3:]: nc.dram_tensor(k, v.shape, mybir.dt.from_np(v.dtype), kind="ExternalInput").ap()
           for k, v in arrays.items()}
    out = nc.dram_tensor("out", (BATCH, 1), F32, kind="ExternalOutput").ap()
    build(nc, aps["dense"], aps["ids_cols"], aps["ids_rows"], [aps[f"tbl_{t}"] for t in range(TABLES)],
          aps["w_pairs"], aps["w_dense_a"], aps["w_dense_b"], aps["b1"], aps["w2"], aps["b2"], aps["w3"], out)
    return run_bass_kernel_spmd(nc, [arrays], core_ids=[0]).results[0]["out"]
```

```python
from contextlib import ExitStack

import numpy as np

import concourse.bass as bass
from concourse import mybir

ALU = mybir.AluOpType
ACT = mybir.ActivationFunctionType
F32 = mybir.dt.float32
F32R = mybir.dt.float32r
I32 = mybir.dt.int32
U32 = mybir.dt.uint32

P = 128
BATCH, DIM, TABLES = 512, 128, 26
TILES = BATCH // P
FEATURES = TABLES + 1
H1, H2 = 512, 256
ROWS = [1250, 1000, 1250, 125000, 12500, 1250, 1000, 1000, 12500, 12500, 1000, 1250, 12500,
        1000, 12500, 1000, 1000, 1250, 12500, 12500, 1250, 1000, 1000, 12500, 1000, 1000]

ONEHOT = [1, 6, 7, 10, 13, 15, 16, 21]
GATHERED = [t for t in range(TABLES) if t not in ONEHOT]
NOH, NG = len(ONEHOT), len(GATHERED)
CHUNKS = 8
OH_P = ROWS[ONEHOT[0]] // CHUNKS
PARTS = 2
SLOT_FEATURE = [0] + [1 + t for t in ONEHOT] + [1 + t for t in GATHERED]
SLOTS = 32
REACH = FEATURES // 2
VECTORS = REACH + 1
QUADS = P // 4
UNITS = [(0, 12, 0), (12, 8, 1), (20, 12, 0)]
REGION_BANKS = [3, 2]
BLOCKS = -(-VECTORS // 4)
GROUP = 4
GROUPS = [list(range(g, min(g + GROUP, NG))) for g in range(0, NG, GROUP)]
RING = 3
WARM_UP = 24
HALVES = 2


def block_partitions(r):
    return 32 * min(4, VECTORS - 4 * r)


def plan_steps():
    groups = [("group", t, g) for t in range(TILES) for g in range(len(GROUPS))]
    steps = [("offset", 0), ("prep", 0, 0), ("prep", 0, 1), ("offset", 1), ("prep", 1, 0), ("prep", 1, 1)]
    for i in range(NOH):
        ahead = [("offset", i + 2), ("prep", i + 2, 0), ("prep", i + 2, 1)] if i + 2 < NOH else []
        steps += ahead[0:2] + [("onehot", i)] + ahead[2:3]
        if i == 0:
            steps.append(("dense",))
        elif i <= 6:
            steps.append(groups.pop(0))

    def take(t, n):
        out = [x for x in groups[:n] if x[1] <= t]
        del groups[:len(out)]
        return out

    def layers(t):
        return [("layer1", t, 0), ("layer1", t, 1), ("layer2", t)]

    for t in range(TILES):
        mine = take(t, len(GROUPS))
        before = layers(t - 1) if t else []
        steps += mine + before[0:1] + [("gram", t, 0), ("gram", t, 1)] + (before[1:2] or take(t + 1, 1))
        steps += [("gram", t, 2)] + take(t + 1, 1) + (before[2:3] or take(t + 1, 2)) + take(t + 1, 1)
    return steps + layers(TILES - 1)


STEPS = plan_steps()


def plan_ring():
    number, emptied_by = {}, {}
    for s in STEPS:
        if s[0] not in ("offset", "prep", "gram"):
            number[s] = len(number)
            emptied_by[s] = "scalar"
            if s[0] == "layer2" or (s[0] == "layer1" and s[2] == 1) or (s[0] == "group" and s[1] and s[2] % 2):
                emptied_by[s] = "vector"
    return number, emptied_by


USE, EMPTIED_BY = plan_ring()
USES = sorted(USE, key=USE.get)


def emptied(engine, last_use):
    return sum(EMPTIED_BY[s] == engine for s in USES[:last_use + 1])


def build(nc, dense, ids_cols, ids_rows, tables, w_pairs, w_dense_a, w_dense_b, b1, w2, b2, w3, out):
    ctx = ExitStack()
    with ctx:
        def sb(name, shape, dt=F32):
            return ctx.enter_context(nc.sbuf_tensor(name, shape, dt))

        def sem(name):
            return ctx.enter_context(nc.semaphore(name))

        idx = sb("idx", [P, TILES * TABLES], I32)
        ids_bc = sb("ids_bc", [P, NOH, BATCH], I32)
        row = sb("row", [P, 1])
        minus_row = sb("minus_row", [P, 1])
        ident = sb("ident", [P, P])
        dense_sb = sb("dense_sb", [P, TILES, DIM])
        gath = sb("gath", [P, 2, NG, DIM])
        xT = sb("xT", [P, BATCH, SLOTS])
        table = sb("table", [P, 3, CHUNKS * DIM])
        parts = sb("parts", [P, 2, PARTS, CHUNKS * DIM], F32R)
        offset = sb("offset", [P, 3, BATCH])
        onehot = sb("onehot", [P, 2, CHUNKS, BATCH], F32R)
        overlaid = sb("overlaid", [P, REACH], I32)
        pairs = sb("pairs", [P, 2, BLOCKS, P])
        wp = sb("wp", [P, BLOCKS, H1])
        wd = sb("wd", [P, 3, H1])
        denseT = sb("denseT", [P, BATCH])
        b1_sb = sb("b1_sb", [P, H1 // P])
        w2_sb = sb("w2_sb", [P, H1 // P, H2])
        b2_bc = sb("b2_bc", [P, H2])
        w3_bc = sb("w3_bc", [P, H2])
        h1T = sb("h1T", [P, 2, H1 // P, P])
        h2 = sb("h2", [P, H2])
        h2w = sb("h2w", [P, H2])
        y = sb("y", [P, TILES])

        bank = [ctx.enter_context(nc.psum_tensor(f"bank{i}", [P, 512], F32)) for i in range(RING)]
        gram = [ctx.enter_context(nc.psum_tensor(f"gram{i}", [P, 4 * banks, P], F32))
                for i, banks in enumerate(REGION_BANKS)]

        idx_loaded = sem("idx_loaded")
        ids_loaded = [sem(f"ids_loaded{i}") for i in range(NOH)]
        table_loaded = [sem(f"table_loaded{i}") for i in range(NOH)]
        dense_loaded = sem("dense_loaded")
        wd_loaded = sem("wd_loaded")
        wp_loaded = sem("wp_loaded")
        b1_loaded = sem("b1_loaded")
        w2_loaded = sem("w2_loaded")
        b2_loaded = sem("b2_loaded")
        w3_loaded = sem("w3_loaded")
        rows_in = [[sem(f"rows_in{p}_{g}") for g in range(len(GROUPS))] for p in range(2)]
        ident_zeroed = sem("ident_zeroed")
        ident_ready = sem("ident_ready")
        row_ready = sem("row_ready")
        minus_row_ready = sem("minus_row_ready")
        pads_zeroed = sem("pads_zeroed")
        wd_summed = sem("wd_summed")
        offset_ready = sem("offset_ready")
        onehots_ready = sem("onehots_ready")
        high_ready = sem("high_ready")
        parts_ready = sem("parts_ready")
        half_used = sem("half_used")
        bank_full = sem("bank_full")
        freed = {"scalar": sem("freed_by_scalar"), "vector": sem("freed_by_vector")}
        gram_full = sem("gram_full")
        base_copied = sem("base_copied")
        mask_filled = sem("mask_filled")
        mask_ready = sem("mask_ready")
        pairs_ready = sem("pairs_ready")
        denseT_copied = sem("denseT_copied")
        h2_biased = sem("h2_biased")
        y_ready = sem("y_ready")
        y_stored = sem("y_stored")

        block = ctx.enter_context(nc.Block())

        @block.sync
        def _(sp):
            sp.dma_start(idx[:], ids_cols).then_inc(idx_loaded, 16)

            def load_ids(i):
                sp.dma_start(ids_bc[0:OH_P, i, :], ids_rows[i:i + 1, :].broadcast_to([OH_P, BATCH])
                             ).then_inc(ids_loaded[i], 16)

            def load_table(i):
                if i >= 3:
                    sp.wait_ge(parts_ready, HALVES * (i - 2))
                sp.dma_start(table[0:OH_P, i % 3, :],
                             tables[ONEHOT[i]].rearrange("(p c) d -> p (c d)", c=CHUNKS)
                             ).then_inc(table_loaded[i], 16)

            load_table(0)
            load_table(1)
            load_ids(1)
            load_table(2)
            load_ids(2)
            sp.dma_start(dense_sb[:], dense).then_inc(dense_loaded, 16)
            sp.dma_start(wd[:, 0, :], w_dense_a).then_inc(wd_loaded, 16)
            sp.dma_start(wd[:, 1, :], w_dense_b).then_inc(wd_loaded, 16)
            sp.dma_start(wp[:, 0:BLOCKS - 1, :], w_pairs[:, 0:BLOCKS - 1, :]).then_inc(wp_loaded, 16)
            last = block_partitions(BLOCKS - 1)
            sp.dma_start(wp[0:last, BLOCKS - 1, :], w_pairs[0:last, BLOCKS - 1, :]).then_inc(wp_loaded, 16)
            for i in range(3, NOH):
                load_ids(i)
                load_table(i)
            sp.dma_start(b1_sb[:], b1).then_inc(b1_loaded, 16)
            sp.dma_start(w2_sb[:], w2).then_inc(w2_loaded, 16)
            sp.dma_start(b2_bc[:], b2.broadcast_to([P, H2])).then_inc(b2_loaded, 16)
            sp.dma_start(w3_bc[:], w3.broadcast_to([P, H2])).then_inc(w3_loaded, 16)
            for t in range(TILES):
                sp.wait_ge(y_ready, t + 1)
                sp.dma_start(out[t * P:(t + 1) * P, :], y[:, t:t + 1]).then_inc(y_stored, 16)
            sp.wait_ge(y_stored, 16 * TILES)

        @block.gpsimd
        def _(pool):
            nc.gpsimd.iota(row[:], [[0, 1]], base=0, channel_multiplier=CHUNKS,
                           allow_small_or_imprecise_dtypes=True).then_inc(row_ready, 1)
            nc.gpsimd.memset(ident[:], 0.0).then_inc(ident_zeroed, 1)
            pool.wait_ge(ident_zeroed, 1)
            nc.gpsimd.affine_select(out=ident[:], in_=ident[:], compare_op=ALU.not_equal, fill=1.0, base=0,
                                    pattern=[[-1, P]], channel_multiplier=1).then_inc(ident_ready, 1)
            for j in range(4):
                mask = overlaid[32 * j:32 * j + 32, :]
                nc.gpsimd.memset(mask, 1).then_inc(mask_filled, 1)
                pool.wait_ge(mask_filled, 3 * j + 1)
                nc.gpsimd.affine_select(out=mask, in_=mask, compare_op=ALU.is_gt, fill=0.0, base=0,
                                        pattern=[[-1, REACH]], channel_multiplier=1).then_inc(mask_filled, 1)
                pool.wait_ge(mask_filled, 3 * j + 2)
                nc.gpsimd.affine_select(out=mask, in_=mask, compare_op=ALU.is_ge, fill=0.0, base=REACH,
                                        pattern=[[1, REACH]], channel_multiplier=-1).then_inc(mask_filled, 1)
                pool.wait_ge(mask_filled, 3 * j + 3)
                pool.sem_inc(mask_ready, 1)
            pool.wait_ge(idx_loaded, 16)
            for t in range(TILES):
                for g, group in enumerate(GROUPS):
                    if t >= 2:
                        pool.wait_ge(bank_full, USE[("group", t - 2, g)] + 1)
                    for s in group:
                        nc.gpsimd.indirect_dma_start(
                            gath[:, t % 2, s, :], None, tables[GATHERED[s]],
                            bass.IndirectOffsetOnAxis(
                                idx[:, t * TABLES + GATHERED[s]:t * TABLES + GATHERED[s] + 1].bitcast(U32), 0),
                        ).then_inc(rows_in[t % 2][g], 16)

        def pair_blocks(s):
            _, t, u = s
            first_quad, quads, region = UNITS[u]
            products = gram[region]
            for j in range(4):
                for k in range(4):
                    base = list(range(k, VECTORS, 4))
                    over = list(range(k, REACH, 4))
                    b0 = 4 * first_quad + j
                    at = slice(b0, b0 + 4 * (quads - 1) + 1, 4)

                    def columns(vectors, shift):
                        c = FEATURES * j + vectors[0] + shift
                        return products[32 * j:32 * j + 32, 0:quads, c:c + 4 * (len(vectors) - 1) + 1:4
                                        ].rearrange("p q r -> p r q")

                    dst = pairs[32 * k:32 * k + 32, t % 2, :, :]
                    mask = overlaid[32 * j:32 * j + 32, k:over[-1] + 1:4].unsqueeze(2).broadcast_to(
                        [32, len(over), quads])
                    yield (dst[:, 0:len(base), at], columns(base, REACH),
                           dst[:, 0:len(over), at], columns(over, 0), mask)

        def feature_bank(s):
            src = bank[USE[s] % RING]
            if s[0] == "dense":
                return xT[:, :, 0], src[:]
            if s[0] == "onehot":
                return xT[:, :, 1 + s[1]], src[:]
            _, t, g = s
            s0, n = 1 + NOH + GROUPS[g][0], len(GROUPS[g])
            return (xT[:, t * P:(t + 1) * P, s0:s0 + n].rearrange("p b s -> p s b"),
                    src[:, 0:n * P].rearrange("p (s b) -> p s b", s=n))

        def hidden(s):
            _, t, half = s
            for n in range(H1 // P // HALVES):
                c = half * (H1 // P // HALVES) + n
                yield h1T[:, t % 2, c, :], bank[USE[s] % RING][:, n * P:(n + 1) * P], b1_sb[:, c:c + 1]

        @block.scalar
        def _(act):
            act.dma_start(ids_bc[0:OH_P, 0, :], ids_rows[0:1, :].broadcast_to([OH_P, BATCH])
                          ).then_inc(ids_loaded[0], 16)
            act.wait_ge(row_ready, 1)
            nc.scalar.activation(minus_row[:], row[:], ACT.Identity, scale=-1.0).then_inc(minus_row_ready, 1)
            act.wait_ge(minus_row_ready, 1)
            for s in STEPS:
                if s in USE and EMPTIED_BY[s] == "scalar":
                    act.wait_ge(bank_full, USE[s] + 1)
                if s[0] == "offset":
                    i = s[1]
                    act.wait_ge(ids_loaded[i], 16)
                    if i >= 3:
                        act.wait_ge(onehots_ready, HALVES * (i - 2))
                    nc.scalar.activation(offset[0:OH_P, i % 3, :], ids_bc[0:OH_P, i, :], ACT.Identity,
                                         bias=minus_row[0:OH_P, :]).then_inc(offset_ready, 1)
                elif s[0] == "prep":
                    _, i, half = s
                    act.wait_ge(table_loaded[i], 16)
                    if i >= 2:
                        if half == 0:
                            act.wait_ge(half_used, i - 1)
                        else:
                            act.wait_ge(bank_full, USE[("onehot", i - 2)] + 1)
                    c = slice(half * CHUNKS * DIM // HALVES, (half + 1) * CHUNKS * DIM // HALVES)
                    nc.scalar.copy(parts[0:OH_P, i % 2, 0, c], table[0:OH_P, i % 3, c]).then_inc(high_ready, 1)
                elif s[0] == "gram":
                    n = len(UNITS) * s[1] + s[2]
                    act.wait_ge(gram_full, n + 1)
                    if s[1] >= 2 and s[2] == 0:
                        act.wait_ge(bank_full, USE[("layer1", s[1] - 2, 1)] + 1)
                    for m, (dst, src, *_) in enumerate(pair_blocks(s)):
                        last = nc.scalar.copy(dst, src)
                        if m % 4 == 3:
                            last.then_inc(base_copied, 1)
                elif s[0] == "layer1" and EMPTIED_BY[s] == "scalar":
                    if s == ("layer1", 0, 0):
                        act.wait_ge(b1_loaded, 16)
                    if s[1] >= 2:
                        act.wait_ge(bank_full, USE[("layer2", s[1] - 2)] + 1)
                    for dst, src, bias in hidden(s):
                        last = nc.scalar.activation(dst, src, ACT.Relu, bias=bias)
                    last.then_inc(freed["scalar"], 1)
                elif s in USE and EMPTIED_BY[s] == "scalar":
                    if s[0] == "dense":
                        nc.scalar.copy(denseT[:], bank[USE[s] % RING][:]).then_inc(denseT_copied, 1)
                    dst, src = feature_bank(s)
                    nc.scalar.copy(dst, src).then_inc(freed["scalar"], 1)

        @block.vector
        def _(dve):
            nc.vector.memset(xT[:, :, FEATURES:SLOTS], 0.0).then_inc(pads_zeroed, 1)
            for s in STEPS:
                if s in USE and EMPTIED_BY[s] == "vector":
                    dve.wait_ge(bank_full, USE[s] + 1)
                if s[0] == "prep":
                    _, i, half = s
                    b = i % 2
                    if half == 0:
                        dve.wait_ge(offset_ready, i + 1)
                    if i >= 2:
                        if half == 0:
                            dve.wait_ge(half_used, i - 1)
                        else:
                            dve.wait_ge(bank_full, USE[("onehot", i - 2)] + 1)
                    for c in range(half * CHUNKS // HALVES, (half + 1) * CHUNKS // HALVES):
                        last = nc.vector.tensor_scalar(onehot[0:OH_P, b, c, :], offset[0:OH_P, i % 3, :], float(c),
                                                       None, ALU.is_equal)
                    last.then_inc(onehots_ready, 1)
                    dve.wait_ge(high_ready, HALVES * i + half + 1)
                    c = slice(half * CHUNKS * DIM // HALVES, (half + 1) * CHUNKS * DIM // HALVES)
                    nc.vector.tensor_tensor(parts[0:OH_P, b, 1, c], table[0:OH_P, i % 3, c],
                                            parts[0:OH_P, b, 0, c].bitcast(F32), ALU.subtract
                                            ).then_inc(parts_ready, 1)
                elif s[0] == "gram":
                    n = len(UNITS) * s[1] + s[2]
                    if n == 0:
                        dve.wait_ge(mask_ready, 4)
                    for m, (_, _, dst, src, mask) in enumerate(pair_blocks(s)):
                        if m % 4 == 0:
                            dve.wait_ge(base_copied, 4 * n + m // 4 + 1)
                        last = nc.vector.copy_predicated(dst, mask, src)
                    last.then_inc(pairs_ready, 1)
                elif s[0] == "layer1" and EMPTIED_BY[s] == "vector":
                    if s == ("layer1", 0, 1):
                        dve.wait_ge(b1_loaded, 16)
                    if s[1] >= 2:
                        dve.wait_ge(bank_full, USE[("layer2", s[1] - 2)] + 1)
                    for dst, src, bias in hidden(s):
                        last = nc.vector.tensor_scalar(dst, src, bias, 0.0, ALU.add, ALU.max)
                    last.then_inc(freed["vector"], 1)
                elif s[0] == "layer2":
                    t = s[1]
                    if t == 0:
                        dve.wait_ge(b2_loaded, 16)
                        dve.wait_ge(w3_loaded, 16)
                    else:
                        dve.wait_ge(y_ready, t)
                    nc.vector.tensor_tensor(h2[:], bank[USE[s] % RING][:, 0:H2], b2_bc[:], ALU.add
                                            ).then_inc(freed["vector"], 1)
                    dve.wait_ge(freed["vector"], emptied("vector", USE[s]))
                    nc.vector.scalar_tensor_tensor(out=h2w[:], in0=h2[:], scalar=0.0, in1=w3_bc[:], op0=ALU.max,
                                                   op1=ALU.mult, accum_out=y[:, t:t + 1]).then_inc(y_ready, 1)
                elif s in USE and EMPTIED_BY[s] == "vector":
                    dst, src = feature_bank(s)
                    nc.vector.tensor_copy(dst, src).then_inc(freed["vector"], 1)
                if s == ("dense",):
                    dve.wait_ge(wd_loaded, 32)
                    nc.vector.tensor_tensor(wd[:, 2, :], wd[:, 0, :], wd[:, 1, :], ALU.add).then_inc(wd_summed, 1)

        @block.tensor
        def _(pe):
            def wait_emptied(last_use):
                for engine in freed:
                    if emptied(engine, last_use):
                        pe.wait_ge(freed[engine], emptied(engine, last_use))

            pe.wait_ge(ident_ready, 1)
            for _ in range(WARM_UP):
                nc.tensor.transpose(bank[0][:, 0:P], ident[:], ident[:])
            for s in STEPS:
                if s in USE:
                    dst = bank[USE[s] % RING]
                    if USE[s] >= RING:
                        wait_emptied(USE[s] - RING)
                if s[0] == "dense":
                    pe.wait_ge(dense_loaded, 16)
                    for t in range(TILES):
                        last = nc.tensor.transpose(dst[:, t * P:(t + 1) * P], dense_sb[:, t, :], ident[:])
                    last.then_inc(bank_full, 1)
                elif s[0] == "onehot":
                    i = s[1]
                    for c in range(CHUNKS):
                        if c % (CHUNKS // HALVES) == 0:
                            half = HALVES * i + c // (CHUNKS // HALVES)
                            pe.wait_ge(onehots_ready, half + 1)
                            pe.wait_ge(parts_ready, half + 1)
                        for part in range(PARTS):
                            last = nc.tensor.matmul(dst[:], parts[0:OH_P, i % 2, part, c * DIM:(c + 1) * DIM],
                                                    onehot[0:OH_P, i % 2, c, :],
                                                    start=(c == 0 and part == 0),
                                                    stop=(c == CHUNKS - 1 and part == PARTS - 1))
                        if c == CHUNKS // HALVES - 1:
                            last.then_inc(half_used, 1)
                    last.then_inc(bank_full, 1)
                elif s[0] == "group":
                    _, t, g = s
                    pe.wait_ge(rows_in[t % 2][g], 16 * len(GROUPS[g]) * (t // 2 + 1))
                    for n, slot in enumerate(GROUPS[g]):
                        last = nc.tensor.transpose(dst[:, n * P:(n + 1) * P], gath[:, t % 2, slot, :], ident[:])
                    last.then_inc(bank_full, 1)
                elif s[0] == "gram":
                    _, t, u = s
                    n = len(UNITS) * t + u
                    if n == 0:
                        pe.wait_ge(pads_zeroed, 1)
                    if u == 0:
                        wait_emptied(max(USE[x] for x in USE if x[0] in ("dense", "onehot") or
                                         (x[0] == "group" and x[1] == t)))
                    first_quad, quads, region = UNITS[u]
                    earlier = [m for m in range(n) if UNITS[m % len(UNITS)][2] == region]
                    if earlier:
                        pe.wait_ge(pairs_ready, earlier[-1] + 1)
                    for q in range(quads):
                        b0 = t * P + 4 * (first_quad + q)
                        quad = xT[:, b0:b0 + 4, :]
                        last = nc.tensor.matmul(gram[region][:, q, 0:4 * FEATURES], quad, quad[:, :, 0:FEATURES],
                                                start=True, stop=True)
                    last.then_inc(gram_full, 1)
                elif s[0] == "layer1":
                    _, t, half = s
                    if t == 0:
                        pe.wait_ge(wd_summed, 1)
                        pe.wait_ge(denseT_copied, 1)
                        pe.wait_ge(wp_loaded, 32)
                    pe.wait_ge(pairs_ready, len(UNITS) * (t + 1))
                    for n in range(H1 // P // HALVES):
                        h = slice((half * (H1 // P // HALVES) + n) * P, (half * (H1 // P // HALVES) + n + 1) * P)
                        to = dst[:, n * P:(n + 1) * P]
                        nc.tensor.matmul(to, wd[:, 2, h], denseT[:, t * P:(t + 1) * P], start=True, stop=False)
                        for r in range(BLOCKS):
                            k = block_partitions(r)
                            last = nc.tensor.matmul(to, wp[0:k, r, h], pairs[0:k, t % 2, r, :],
                                                    start=False, stop=(r == BLOCKS - 1))
                    last.then_inc(bank_full, 1)
                elif s[0] == "layer2":
                    t = s[1]
                    if t == 0:
                        pe.wait_ge(w2_loaded, 16)
                    for c in range(H1 // P):
                        if c % (H1 // P // HALVES) == 0:
                            half = ("layer1", t, c // (H1 // P // HALVES))
                            pe.wait_ge(freed[EMPTIED_BY[half]], emptied(EMPTIED_BY[half], USE[half]))
                        last = nc.tensor.matmul(dst[:, 0:H2], h1T[:, t % 2, c, :], w2_sb[:, c, :],
                                                start=(c == 0), stop=(c == H1 // P - 1))
                    last.then_inc(bank_full, 1)


def pair_rows():
    first = np.cumsum([0] + [FEATURES - 1 - f for f in range(FEATURES - 1)])
    rows = np.full((P, BLOCKS), -1)
    for m in range(VECTORS):
        for slot in range(FEATURES):
            column = m if m < slot <= m + REACH and m < REACH else m + REACH
            if (slot - column) % FEATURES in range(1, REACH + 1):
                lo, hi = sorted((SLOT_FEATURE[slot], SLOT_FEATURE[column]))
                rows[32 * (m % 4) + slot, m // 4] = DIM + first[lo] + hi - lo - 1
    assert sorted(rows[rows >= 0]) == list(range(DIM, DIM + FEATURES * REACH))
    return rows


def kernel(**inputs):
    import concourse.bacc as bacc
    from concourse.bass_utils import run_bass_kernel_spmd

    w1 = np.asarray(inputs["W_top1"])
    ids = np.asarray(inputs["ids"])
    rows = pair_rows()
    w_pairs = np.zeros((P, BLOCKS, H1), w1.dtype)
    w_pairs[rows >= 0] = w1[rows[rows >= 0]]
    arrays = {
        "dense": np.asarray(inputs["r_dense_features"]).reshape(TILES, P, DIM).transpose(1, 0, 2),
        "ids_cols": ids.reshape(TILES, P, TABLES).transpose(1, 0, 2).reshape(P, TILES * TABLES),
        "ids_rows": ids.T[ONEHOT],
        **{f"tbl_{t}": np.asarray(inputs[f"tbl_{t}"]) for t in range(TABLES)},
        "w_pairs": w_pairs,
        "w_dense_a": w1[:DIM],
        "w_dense_b": w1[-DIM:],
        "b1": np.asarray(inputs["b_top1"]).reshape(H1 // P, P).T,
        "w2": np.asarray(inputs["W_top2"]).reshape(H1 // P, P, H2).transpose(1, 0, 2),
        "b2": np.asarray(inputs["b_top2"]).reshape(1, H2),
        "w3": np.asarray(inputs["W_top3"]).reshape(1, H2),
    }
    arrays = {f"in_{k}": np.ascontiguousarray(v) for k, v in arrays.items()}
    nc = bacc.Bacc("TRN2", target_bir_lowering=False, num_devices=1)
    aps = {k[3:]: nc.dram_tensor(k, v.shape, mybir.dt.from_np(v.dtype), kind="ExternalInput").ap()
           for k, v in arrays.items()}
    out = nc.dram_tensor("out", (BATCH, 1), F32, kind="ExternalOutput").ap()
    build(nc, aps["dense"], aps["ids_cols"], aps["ids_rows"], [aps[f"tbl_{t}"] for t in range(TABLES)],
          aps["w_pairs"], aps["w_dense_a"], aps["w_dense_b"], aps["b1"], aps["w2"], aps["b2"], aps["w3"], out)
    return run_bass_kernel_spmd(nc, [arrays], core_ids=[0]).results[0]["out"]
```
